# Optimizing a Trainium2 kernel written in Bass

```python
import numpy as np
import jax
import jax.numpy as jnp

def _softmax(x, axis=-1):
    return jax.nn.softmax(x, axis=axis)

def _gelu(x):
    return jax.nn.gelu(x, approximate=True)

def _silu(x):
    return jax.nn.silu(x)

def _sigmoid(x):
    return jax.nn.sigmoid(x)

def _layernorm(x, axis=-1, eps=1e-05):
    m = jnp.mean(x, axis=axis, keepdims=True)
    v = jnp.var(x, axis=axis, keepdims=True)
    return (x - m) / jnp.sqrt(v + eps)

def _scatter_add(tgt, idx, src, axis=0):
    return tgt.at[idx].add(src)

def _segment_sum(src, seg, n):
    return jax.ops.segment_sum(src, seg, n)
kernel_name = 'mk_adj_preln_d4_adj_r2_ef943c'

def setup_inputs(seed: int=0):
    np.random.seed(seed)
    _w = jnp.asarray

    def _rec_inputs():
        import jax
        import jax.numpy as jnp
        _gk = jax.random.key(seed)
        x = -0.000929 + 1 * jax.random.normal(jax.random.fold_in(_gk, 1), (8192, 64), jnp.float32)
        _a = jax.random.bernoulli(jax.random.fold_in(_gk, 2), 0.000488281, (8192, 8192))
        _a = jnp.logical_or(_a, jnp.eye(8192, dtype=bool))
        _af = _a.astype(jnp.float32)
        _af = _af * jax.random.uniform(jax.random.fold_in(_gk, 3), (8192, 8192), jnp.float32, 0.05, 1)
        adj = _af
        return (x, adj)
    x, adj = _rec_inputs()

    def _L0_gnn_setup():
        import jax, jax.numpy as jnp
        import numpy as np
        P_DROP = 0.1
        key = jax.random.key(seed)
        k1, k2, k3 = jax.random.split(key, 3)
        N, D = (8192, 64)
        x = jax.random.normal(k1, (N, D), dtype=jnp.float32)
        adj = jax.random.uniform(k2, (N, N), dtype=jnp.float32)
        u = jax.random.uniform(k3, (N, D), dtype=jnp.float32)
        return {'x': x, 'adj': adj, 'u': u}
    _L0_gnn_all = _L0_gnn_setup()
    _L0_gnn_in = {k: v for k, v in _L0_gnn_all.items() if k in ('u',)}
    del _L0_gnn_all

    def _L1_gnn_setup():
        import jax, jax.numpy as jnp
        import numpy as np
        N, D_IN, D_OUT = (8192, 64, 64)
        AVG_DEG = 32.0
        L2_EPS = 1e-12
        key = jax.random.key(seed)
        kx, ka, kw, kb = jax.random.split(key, 4)
        X = jax.random.normal(kx, (N, D_IN), dtype=jnp.float32)
        adj = (jax.random.uniform(ka, (N, N)) < AVG_DEG / N).astype(jnp.float32)
        bound = 1.0 / np.sqrt(2 * D_IN)
        W = jax.random.uniform(kw, (2 * D_IN, D_OUT), dtype=jnp.float32, minval=-bound, maxval=bound)
        b = jax.random.uniform(kb, (D_OUT,), dtype=jnp.float32, minval=-bound, maxval=bound)
        return {'X': X, 'adj': adj, 'W': W, 'b': b}
    _L1_gnn_all = _L1_gnn_setup()
    _L1_gnn_in = {k: v for k, v in _L1_gnn_all.items() if k in ('W', 'b')}
    del _L1_gnn_all

    def _L2_gnn_setup():
        import jax, jax.numpy as jnp
        import numpy as np
        N = 8192
        IN_C = 64
        OUT_C = 64
        key = jax.random.key(seed)
        k1, k2, k3 = jax.random.split(key, 3)
        g_data = jax.random.normal(k1, (N, IN_C), dtype=jnp.float32)
        g_adj = jax.random.uniform(k2, (N, N), dtype=jnp.float32)
        bound = 1.44 * np.sqrt(6.0 / (IN_C + OUT_C))
        W = jax.random.uniform(k3, (IN_C, OUT_C), dtype=jnp.float32, minval=-bound, maxval=bound)
        return {'g_data': g_data, 'g_adj': g_adj, 'W': W}
    _L2_gnn_all = _L2_gnn_setup()
    _L2_gnn_in = {k: v for k, v in _L2_gnn_all.items() if k in ('W',)}
    del _L2_gnn_all

    def _L3_gnn_setup():
        import jax, jax.numpy as jnp
        import numpy as np
        N = 8192
        F = 64
        O = 64
        key = jax.random.key(seed)
        k1, k2, k3 = jax.random.split(key, 3)
        features = jax.random.normal(k1, (N, F), dtype=jnp.float32)
        adj = jax.random.uniform(k2, (N, N), dtype=jnp.float32)
        W = jax.random.normal(k3, (O, 2 * F), dtype=jnp.float32)
        return {'features': features, 'adj': adj, 'W': W}
    _L3_gnn_all = _L3_gnn_setup()
    _L3_gnn_in = {k: v for k, v in _L3_gnn_all.items() if k in ('W',)}
    del _L3_gnn_all
    return {'x': x, 'adj': adj, 'L0_gnn_u': _L0_gnn_in['u'], 'L1_gnn_W': _L1_gnn_in['W'], 'L1_gnn_b': _L1_gnn_in['b'], 'L2_gnn_W': _L2_gnn_in['W'], 'L3_gnn_W': _L3_gnn_in['W']}

def reference(x, adj, L0_gnn_u, L1_gnn_W, L1_gnn_b, L2_gnn_W, L3_gnn_W):
    import jax
    import jax.numpy as jnp

    def _L0_gnn_ref(x, adj, u):
        import jax, jax.numpy as jnp
        import numpy as np
        P_DROP = 0.1
        keep = (u >= P_DROP).astype(x.dtype)
        x_drop = x * keep / (1.0 - P_DROP)
        return jnp.matmul(adj, x_drop)

    def _L1_gnn_ref(X, adj, W, b):
        import jax, jax.numpy as jnp
        import numpy as np
        N, D_IN, D_OUT = (8192, 64, 64)
        AVG_DEG = 32.0
        L2_EPS = 1e-12
        deg = jnp.clip(jnp.sum(adj, axis=1, keepdims=True) + 1.0, 1.0, None)
        h_neigh = (adj @ X + X) / deg
        concat = jnp.concatenate([X, h_neigh], axis=1)
        z = concat @ W + b
        out = jax.nn.relu(z)
        norm = jnp.linalg.norm(out, axis=1, keepdims=True)
        return out / jnp.maximum(norm, L2_EPS)

    def _L2_gnn_ref(g_data, g_adj, W):
        import jax, jax.numpy as jnp
        import numpy as np
        N = 8192
        IN_C = 64
        OUT_C = 64
        n = g_adj.shape[0]
        a = g_adj + jnp.eye(n, dtype=g_adj.dtype)
        deg = a.sum(axis=1)
        dinv = jnp.where(deg > 0, deg ** (-0.5), 0.0)
        a_norm = dinv[:, None] * a * dinv[None, :]
        out = a_norm @ g_data
        out = out @ W
        return out

    def _L3_gnn_ref(features, adj, W):
        import jax, jax.numpy as jnp
        import numpy as np
        N = 8192
        F = 64
        O = 64
        deg = jnp.sum(adj, axis=1, keepdims=True)
        neigh = adj @ features / (deg + 1.0)
        data = jnp.concatenate([features, neigh], axis=-1)
        return data @ W.T
    h = jnp.maximum(_layernorm(x, axis=-1), 0.0)
    x = x + _L0_gnn_ref(h, adj, L0_gnn_u)
    h = jnp.maximum(_layernorm(x, axis=-1), 0.0)
    x = x + _L1_gnn_ref(h, adj, L1_gnn_W, L1_gnn_b)
    h = jnp.maximum(_layernorm(x, axis=-1), 0.0)
    x = x + _L2_gnn_ref(h, adj, L2_gnn_W)
    h = jnp.maximum(_layernorm(x, axis=-1), 0.0)
    x = x + _L3_gnn_ref(h, adj, L3_gnn_W)
    return x

_drawn_inputs = setup_inputs


def setup_inputs(seed=0):
    import zlib

    import numpy as np

    out = dict(_drawn_inputs(seed))
    spreads = {}
    factors = {'L1_gnn_b': 4.111}
    for name, (base, spread) in spreads.items():
        noise = np.random.default_rng([zlib.crc32(name.encode()), seed]).standard_normal(out[name].shape)
        drawn = base * np.exp(spread * noise) if base else spread * noise
        out[name] = jnp.asarray(drawn.astype(out[name].dtype))
    for name, factor in factors.items():
        out[name] = (out[name] * factor).astype(out[name].dtype)
    return out
```

```python
from contextlib import ExitStack

import concourse.bass as bass
from concourse import mybir

N = 8192
F = 64
P = 128
TILES = N // P
BLOCK_TILES = 8
BLOCKS = TILES // BLOCK_TILES
COLS = BLOCK_TILES * P
BANK = 512
BANKS = COLS // BANK
FEATS = BLOCK_TILES * F

CHUNK_TILES = 2
CHUNKS = 30
RING = 5
LOADS = CHUNKS // RING
SINGLE = CHUNKS * CHUNK_TILES
CACHED = TILES - SINGLE - 1
FIRST_CACHED = SINGLE + 1
MIDDLE = CHUNKS // 2

LAYERS = 4
P_DROP = 0.1
LN_EPS = 1e-5
L2_EPS = 1e-12
LEAST_DEGREE = 2.0 ** -100

HAS_SELF = (False, True, True, False)
HAS_TOP = (False, True, False, True)
SUMS_DEGREE = (True, True, False, False)

PROLOGUE_STEPS, EPILOGUE_STEPS = 8, (8, 19, 8, 3)
PROLOGUE_ROOTS, EPILOGUE_ROOTS = 1, (1, 2, 1, 0)


def gnn_stack(nc, x_in, stream_in, single_in, cached_in, u_in, w1_in, b1_in, w2_in, w3_in, x_out):
    fp32 = mybir.dt.float32
    ALU = mybir.AluOpType
    ACT = mybir.ActivationFunctionType
    X = mybir.AxisListType.X

    ctx = ExitStack()
    with ctx:
        def sbuf(name, shape):
            return ctx.enter_context(nc.sbuf_tensor(name, shape, fp32))

        def psum(name, shape):
            return ctx.enter_context(nc.psum_tensor(name, shape, fp32))

        def sem(name):
            return ctx.enter_context(nc.semaphore(name))

        x = sbuf("x", [P, TILES * F])
        h = [sbuf(f"h{i}", [P, TILES * F]) for i in range(2)]
        u = h[1]
        ring = [sbuf(f"ring{i}", [P, CHUNK_TILES * COLS]) for i in range(RING)]
        single = sbuf("single", [P, COLS])
        cache = sbuf("cache", [P, BLOCKS * CACHED * COLS])
        y_sb = sbuf("y_sb", [P, COLS])
        own_h = sbuf("own_h", [P, FEATS])
        own_hT = sbuf("own_hT", [P, COLS])
        row_sum = sbuf("row_sum", [P, COLS])
        ident = sbuf("ident", [P, P])
        ones = sbuf("ones", [P, 1])
        below = sbuf("below", [P, LAYERS, F])
        above = sbuf("above", [P, LAYERS, F])
        squares, z_sb = row_sum[:, 0:FEATS], row_sum[:, FEATS:2 * FEATS]
        mean = sbuf("mean", [P, BLOCK_TILES])
        to_root = sbuf("to_root", [P, 2 * BLOCK_TILES])
        rooted = sbuf("rooted", [P, 2 * BLOCK_TILES])
        inverse = sbuf("inverse", [P, 2 * BLOCK_TILES])
        inv_deg = sbuf("inv_deg", [P, BLOCK_TILES])
        degree = sbuf("degree", [P, TILES])
        deg_rsqrt = sbuf("deg_rsqrt", [P, TILES])

        Y = psum("Y", [P, COLS])
        HT = psum("HT", [P, COLS])
        Z = psum("Z", [P, FEATS])
        TOP = psum("TOP", [P, FEATS])
        DEG = psum("DEG", [P, BANK])

        x_loaded = [sem(f"x_loaded{i}") for i in range(4)]
        weights_loaded = sem("weights_loaded")
        weights_clear = sem("weights_clear")
        consts_ready = sem("consts_ready")
        chunk_loaded = [sem(f"chunk_loaded{i}") for i in range(RING)]
        single_loaded = sem("single_loaded")
        cache_loaded = sem("cache_loaded")
        chunk_multiplied = sem("chunk_multiplied")
        chunk_summed = sem("chunk_summed")
        single_multiplied = sem("single_multiplied")
        rest_summed = sem("rest_summed")
        h_blocks = sem("h_blocks")
        own_h_ready = sem("own_h_ready")
        hT_done = sem("hT_done")
        hT_copied = sem("hT_copied")
        y_done = sem("y_done")
        y_copied = sem("y_copied")
        z_done = sem("z_done")
        root_asked = sem("root_asked")
        root_done = sem("root_done")
        dve_step = sem("dve_step")
        gp_step = sem("gp_step")
        out_stored = sem("out_stored")

        block = ctx.enter_context(nc.Block())

        def own(buf, b):
            return buf[:, bass.ds(b * FEATS, FEATS)]

        def by_tile(ap):
            return ap.rearrange("p (t f) -> p t f", f=F)

        def spread(ap):
            return ap.unsqueeze(2).to_broadcast([P, BLOCK_TILES, F])

        @block.sync
        def _(sp):
            def load_block(layer, b):
                blocks = layer * BLOCKS + b
                for c in range(CHUNKS):
                    before = blocks * CHUNKS + c
                    sp.wait_ge(chunk_multiplied, before + 1)
                    if SUMS_DEGREE[layer]:
                        sp.wait_ge(chunk_summed, before + 1)
                    elif SUMS_DEGREE[layer - 1] and c < RING:
                        sp.wait_ge(chunk_summed, layer * BLOCKS * CHUNKS + c + 1)
                    sp.dma_start(ring[c % RING][:, :], stream_in[b, c]).then_inc(chunk_loaded[c % RING], 16)
                sp.wait_ge(single_multiplied, blocks + 1)
                if layer == 0:
                    sp.wait_ge(rest_summed, 2 * b + 1)
                elif layer == 1:
                    sp.wait_ge(rest_summed, 2 * BLOCKS + 1)
                sp.dma_start(single[:, :], single_in[b]).then_inc(single_loaded, 16)
                if layer == 0:
                    sp.dma_start(cache[:, bass.ds(b * CACHED * COLS, CACHED * COLS)],
                                 cached_in[b]).then_inc(cache_loaded, 16)

            for layer in range(LAYERS):
                with sp.Fori(0, BLOCKS) as b:
                    load_block(layer, b)

        @block.gpsimd
        def _(gp):
            nc.gpsimd.memset(above[:, :, :], 0.0).then_inc(weights_clear, 1)
            nc.gpsimd.memset(ident[:, :], 0.0)
            nc.gpsimd.memset(ones[:, :], 1.0)
            nc.gpsimd.memset(below[:, 0, :], 0.0).then_inc(gp_step, 1)
            gp.wait_ge(gp_step, 1)
            nc.gpsimd.affine_select(out=ident[:, :], in_=ident[:, :], compare_op=ALU.not_equal, fill=1.0,
                                    base=0, pattern=[[-1, P]], channel_multiplier=1)
            nc.gpsimd.affine_select(out=below[:, 0, :], in_=below[:, 0, :], compare_op=ALU.not_equal,
                                    fill=1.0, base=0, pattern=[[-1, F]],
                                    channel_multiplier=1).then_inc(gp_step, 1)
            gp.wait_ge(gp_step, 2)
            nc.gpsimd.affine_select(out=below[:, 0, :], in_=below[:, 0, :], compare_op=ALU.not_equal,
                                    fill=1.0, base=-F, pattern=[[-1, F]],
                                    channel_multiplier=1).then_inc(consts_ready, 1)

            for layer in range(1, LAYERS):
                with gp.Fori(0, BLOCKS) as b:
                    gp.wait_ge(h_blocks, layer * BLOCKS + b + 1)
                    gp.wait_ge(y_done, (layer * BLOCKS + b) * BANKS)
                    nc.gpsimd.tensor_copy(own_h[:, :], own(h[layer % 2], b)).then_inc(own_h_ready, 1)
                    if layer == LAYERS - 1:
                        gp.wait_ge(h_blocks, (layer + 1) * BLOCKS + b + 1)
                        gp.dma_start(x_out[:, bass.ds(b * FEATS, FEATS)], own(x, b)).then_inc(out_stored, 16)
            gp.wait_ge(out_stored, 16 * BLOCKS)

        @block.scalar
        def _(act):
            quarter = TILES * F // 4
            for q in range(4):
                part = slice(q * quarter, (q + 1) * quarter)
                act.dma_start(x[:, part], x_in[:, part]).then_inc(x_loaded[q], 16)
                act.dma_start(u[:, part], u_in[:, part]).then_inc(x_loaded[q], 16)
            act.wait_ge(weights_clear, 1)
            act.dma_start(above[0:F, 1, :], w1_in[0:F, :]).then_inc(weights_loaded, 16)
            act.dma_start(above[F:F + 1, 1, :], b1_in).then_inc(weights_loaded, 16)
            act.dma_start(above[0:F, 3, :], w3_in[0:F, :]).then_inc(weights_loaded, 16)
            for half in (slice(0, F), slice(F, 2 * F)):
                act.dma_start(below[half, 1, :], w1_in[F:2 * F, :]).then_inc(weights_loaded, 16)
                act.dma_start(below[half, 2, :], w2_in).then_inc(weights_loaded, 16)
                act.dma_start(below[half, 3, :], w3_in[F:2 * F, :]).then_inc(weights_loaded, 16)

            def root(number):
                act.wait_ge(root_asked, number)
                nc.scalar.activation(rooted[:, :], to_root[:, :], ACT.Sqrt).then_inc(root_done, 1)

            with act.Fori(0, BLOCKS) as b:
                root(b + 1)
            roots, tops = BLOCKS * PROLOGUE_ROOTS, 0
            for layer in range(LAYERS):
                with act.Fori(0, BLOCKS) as b:
                    if HAS_TOP[layer]:
                        act.wait_ge(hT_done, tops + b + 1)
                        for k in range(BANKS):
                            cols = slice(k * BANK, (k + 1) * BANK)
                            nc.scalar.copy(own_hT[0:F, cols], HT[0:F, cols]).then_inc(hT_copied, 1)
                    for k in range(BANKS):
                        act.wait_ge(y_done, (layer * BLOCKS + b) * BANKS + k + 1)
                        cols = slice(k * BANK, (k + 1) * BANK)
                        nc.scalar.copy(y_sb[:, cols], Y[:, cols]).then_inc(y_copied, 1)
                    for r in range(EPILOGUE_ROOTS[layer]):
                        root(roots + b * EPILOGUE_ROOTS[layer] + r + 1)
                roots += BLOCKS * EPILOGUE_ROOTS[layer]
                tops += BLOCKS * HAS_TOP[layer]

        @block.tensor
        def _(pe):
            def multiply(h_now, tiles, first, last, place):
                done = []
                for k in range(BANKS):
                    for J, cols, half in tiles:
                        mm = nc.tensor.matmul(
                            Y[half * F:(half + 1) * F, k * BANK:(k + 1) * BANK],
                            h_now[:, J * F:(J + 1) * F], place(cols, k), start=first, stop=last)
                    done.append(mm)
                return done

            def fixed(buf, k):
                return buf[:, k * BANK:(k + 1) * BANK]

            def own_part(layer, tops, b):
                pe.wait_ge(own_h_ready, (layer - 1) * BLOCKS + b + 1)
                for t in range(BLOCK_TILES):
                    cols = slice(t * P, (t + 1) * P)
                    if HAS_SELF[layer]:
                        nc.tensor.matmul(Y[0:F, cols], own_h[:, t * F:(t + 1) * F], ident[:, :],
                                         start=False, stop=False)
                if HAS_TOP[layer]:
                    for t in range(BLOCK_TILES):
                        cols = slice(t * P, (t + 1) * P)
                        mm = nc.tensor.matmul(HT[0:F, cols], own_h[:, t * F:(t + 1) * F], ident[:, :],
                                              start=True, stop=True)
                    mm.then_inc(hT_done, 1)

            def one_block(layer, tops, b):
                h_now = h[layer % 2]
                blocks = layer * BLOCKS + b
                for c in range(CHUNKS):
                    J = c * CHUNK_TILES
                    if J % BLOCK_TILES == 0:
                        pe.wait_ge(h_blocks, layer * BLOCKS + J // BLOCK_TILES + 1)
                    if c == MIDDLE and (HAS_SELF[layer] or HAS_TOP[layer]):
                        own_part(layer, tops, b)
                    pe.wait_ge(chunk_loaded[c % RING], (blocks * LOADS + c // RING + 1) * 16)
                    buf = ring[c % RING]
                    tiles = [(J + n, buf[:, n * COLS:(n + 1) * COLS], n) for n in range(CHUNK_TILES)]
                    multiply(h_now, tiles, c == 0, False, fixed)[-1].then_inc(chunk_multiplied, 1)
                pe.wait_ge(single_loaded, (blocks + 1) * 16)
                multiply(h_now, [(SINGLE, single, 1)], False, True, fixed)[-1].then_inc(single_multiplied, 1)
                if layer == 0:
                    pe.wait_ge(cache_loaded, (b + 1) * 16)
                for n in range(CACHED):
                    def kept(_, k):
                        return cache[:, bass.ds((b * CACHED + n) * COLS + k * BANK, BANK)]
                    done = multiply(h_now, [(FIRST_CACHED + n, cache, 0)], False, n == CACHED - 1, kept)
                for mm in done:
                    mm.then_inc(y_done, 1)

                pe.wait_ge(h_blocks, blocks + BLOCKS)
                if SUMS_DEGREE[layer]:
                    pe.wait_ge(rest_summed, 2 * blocks + 3)
                    for t in range(BLOCK_TILES):
                        nc.tensor.matmul(DEG[:, t:t + 1], row_sum[:, t * P:(t + 1) * P], ones[:, :],
                                         start=True, stop=True)
                if HAS_TOP[layer]:
                    pe.wait_ge(hT_copied, (tops + b + 1) * BANKS)
                    for t in range(BLOCK_TILES):
                        nc.tensor.matmul(TOP[:, t * F:(t + 1) * F], own_hT[:, t * P:(t + 1) * P],
                                         above[:, layer, :], start=True, stop=True)
                for t in range(BLOCK_TILES):
                    if t * P % BANK == 0:
                        pe.wait_ge(y_copied, blocks * BANKS + t * P // BANK + 1)
                    mm = nc.tensor.matmul(Z[:, t * F:(t + 1) * F], y_sb[:, t * P:(t + 1) * P],
                                          below[:, layer, :], start=True, stop=True)
                mm.then_inc(z_done, 1)

            pe.wait_ge(consts_ready, 2)
            pe.wait_ge(weights_loaded, 9 * 16)
            tops = 0
            for layer in range(LAYERS):
                with pe.Fori(0, BLOCKS) as b:
                    one_block(layer, tops, b)
                tops += BLOCKS * HAS_TOP[layer]

        @block.vector
        def _(dve):
            nc.vector.memset(mean[:, 0:1], 0.0).then_inc(chunk_multiplied, RING)
            nc.vector.memset(mean[:, 1:2], 0.0).then_inc(chunk_summed, RING)
            nc.vector.memset(mean[:, 2:3], 0.0).then_inc(single_multiplied, 1)
            nc.vector.memset(mean[:, 3:4], 0.0).then_inc(rest_summed, 1)
            nc.vector.memset(to_root[:, :], 1.0).then_inc(dve_step, 1)
            nc.vector.memset(own_hT[:, :], 0.0).then_inc(dve_step, 1)
            dve.wait_ge(dve_step, 2)
            nc.vector.memset(own_hT[F:F + 1, :], 1.0).then_inc(consts_ready, 1)

            class Chain:

                def __init__(self, before):
                    self.before, self.steps = before, 0

                def __call__(self, instruction):
                    self.steps += 1
                    instruction.then_inc(dve_step, 1)
                    dve.wait_ge(dve_step, self.before + self.steps)

            def ask_roots(chain, roots):
                dve.wait_ge(root_done, roots)

            def add(chain, out, a, c):
                chain(nc.vector.tensor_tensor(out, a, c, ALU.add))

            def copy(chain, out, a):
                chain(nc.vector.tensor_scalar(out, a, 1.0, None, ALU.mult))

            def new_state(chain, xs, z):
                add(chain, z_sb, z, xs)
                copy(chain, xs, z_sb)

            def layer_norm(chain, hs, roots, scale=None, last=None):
                c3, s3 = by_tile(z_sb), by_tile(squares)
                first = slice(0, BLOCK_TILES)
                chain(nc.vector.tensor_reduce(mean[:, :], c3, X, ALU.add))
                chain(nc.vector.scalar_tensor_tensor(out=c3, in0=spread(mean[:, :]), scalar=-1.0 / F, in1=c3,
                                                     op0=ALU.mult, op1=ALU.add))
                chain(nc.vector.tensor_tensor(squares, z_sb, z_sb, ALU.mult))
                chain(nc.vector.tensor_reduce(inverse[:, first], s3, X, ALU.add))
                nc.vector.tensor_scalar(to_root[:, first], inverse[:, first], 1.0 / F, LN_EPS, ALU.mult,
                                        ALU.add).then_inc(root_asked, 1)
                dve.wait_ge(root_done, roots)
                chain(nc.vector.reciprocal(inverse[:, first], rooted[:, first]))
                if scale is not None:
                    chain(scale(inverse[:, first]))
                done = nc.vector.scalar_tensor_tensor(out=by_tile(hs), in0=c3, scalar=0.0,
                                                      in1=spread(inverse[:, first]), op0=ALU.max, op1=ALU.mult)
                if last is None:
                    done.then_inc(h_blocks, 1)
                else:
                    chain(done)
                    last().then_inc(h_blocks, 1)

            def block_ended(count):
                dve.wait_ge(h_blocks, count)

            def prologue(b, chain):
                copy(chain, z_sb, own(x, b))
                layer_norm(chain, own(h[0], b), b + 1,
                           scale=lambda r: nc.vector.tensor_scalar(r, r, 1.0 / (1.0 - P_DROP), None, ALU.mult),
                           last=lambda: nc.vector.scalar_tensor_tensor(
                               out=own(h[0], b), in0=own(u, b), scalar=P_DROP, in1=own(h[0], b),
                               op0=ALU.is_ge, op1=ALU.mult))

            def sum_tiles(layer, b):
                blocks = layer * BLOCKS + b
                for c in range(CHUNKS):
                    dve.wait_ge(chunk_loaded[c % RING], (blocks * LOADS + c // RING + 1) * 16)
                    tile = ring[c % RING][:, layer * COLS:(layer + 1) * COLS]
                    if c == 0:
                        nc.vector.tensor_copy(row_sum[:, :], tile).then_inc(chunk_summed, 1)
                    else:
                        dve.wait_ge(chunk_summed, blocks * CHUNKS + c + RING)
                        nc.vector.tensor_tensor(row_sum[:, :], row_sum[:, :], tile, ALU.add).then_inc(chunk_summed, 1)
                dve.wait_ge(chunk_summed, (blocks + 1) * CHUNKS + RING)
                if layer == 0:
                    dve.wait_ge(single_loaded, (b + 1) * 16)
                    dve.wait_ge(cache_loaded, (b + 1) * 16)
                kept = [cache[:, bass.ds((b * CACHED + n) * COLS, COLS)] for n in range(CACHED)]
                for n, tile in enumerate([single[:, :], kept[0]] if layer == 0 else kept[1:]):
                    if n:
                        dve.wait_ge(rest_summed, 2 * blocks + n + 1)
                    nc.vector.tensor_tensor(row_sum[:, :], row_sum[:, :], tile, ALU.add).then_inc(rest_summed, 1)

            def epilogue(layer, b, chain, roots):
                blocks = layer * BLOCKS + b
                xs, hs = own(x, b), own(h[(layer + 1) % 2], b)
                z, z3, Z3, s3 = z_sb, by_tile(z_sb), by_tile(Z[:, :]), by_tile(squares)
                deg, rsq = (a[:, bass.ds(b * BLOCK_TILES, BLOCK_TILES)] for a in (degree, deg_rsqrt))
                lo, hi = slice(0, BLOCK_TILES), slice(BLOCK_TILES, 2 * BLOCK_TILES)
                dve.wait_ge(z_done, blocks + 1)
                if layer == 0:
                    copy(chain, deg, DEG[:, lo])
                    new_state(chain, xs, Z[:, :])
                    layer_norm(chain, hs, roots + 1)
                elif layer == 1:
                    chain(nc.vector.scalar_tensor_tensor(out=deg, in0=DEG[:, lo], scalar=1.0, in1=deg,
                                                         op0=ALU.add, op1=ALU.add))
                    chain(nc.vector.tensor_scalar(inv_deg[:, :], deg, 1.0, None, ALU.max))
                    chain(nc.vector.reciprocal(inv_deg[:, :], inv_deg[:, :]))
                    chain(nc.vector.tensor_tensor(z3, Z3, spread(inv_deg[:, :]), ALU.mult))
                    add(chain, z, TOP[:, :], z)
                    chain(nc.vector.scalar_tensor_tensor(out=squares, in0=z, scalar=0.0, in1=z,
                                                         op0=ALU.max, op1=ALU.mult))
                    chain(nc.vector.tensor_reduce(mean[:, :], s3, X, ALU.add))
                    chain(nc.vector.tensor_scalar(to_root[:, lo], mean[:, :], L2_EPS ** 2, None, ALU.max))
                    nc.vector.tensor_scalar(to_root[:, hi], deg, LEAST_DEGREE, None,
                                            ALU.max).then_inc(root_asked, 1)
                    dve.wait_ge(root_done, roots + 1)
                    chain(nc.vector.reciprocal(inverse[:, :], rooted[:, :]))
                    chain(nc.vector.scalar_tensor_tensor(out=rsq, in0=deg, scalar=0.0, in1=inverse[:, hi],
                                                         op0=ALU.is_gt, op1=ALU.mult))
                    chain(nc.vector.scalar_tensor_tensor(out=z3, in0=z3, scalar=0.0,
                                                         in1=spread(inverse[:, lo]), op0=ALU.max, op1=ALU.mult))
                    new_state(chain, xs, z)
                    layer_norm(chain, hs, roots + 2,
                               scale=lambda r: nc.vector.tensor_tensor(r, r, rsq, ALU.mult))
                elif layer == 2:
                    chain(nc.vector.tensor_tensor(z3, Z3, spread(rsq), ALU.mult))
                    new_state(chain, xs, z)
                    layer_norm(chain, hs, roots + 1)
                else:
                    chain(nc.vector.reciprocal(inv_deg[:, :], deg))
                    chain(nc.vector.tensor_tensor(z3, Z3, spread(inv_deg[:, :]), ALU.mult))
                    add(chain, z, TOP[:, :], z)
                    nc.vector.tensor_tensor(xs, z, xs, ALU.add).then_inc(h_blocks, 1)

            steps, roots = 2, 0
            for half in range(4):
                dve.wait_ge(x_loaded[half], 32)
            with dve.Fori(0, BLOCKS) as b:
                chain = Chain(steps + b * PROLOGUE_STEPS)
                prologue(b, chain)
                block_ended(b + 1)
                assert chain.steps == PROLOGUE_STEPS, chain.steps
            steps += BLOCKS * PROLOGUE_STEPS
            roots += BLOCKS * PROLOGUE_ROOTS
            for layer in range(LAYERS):
                with dve.Fori(0, BLOCKS) as b:
                    if SUMS_DEGREE[layer]:
                        sum_tiles(layer, b)
                    chain = Chain(steps + b * EPILOGUE_STEPS[layer])
                    epilogue(layer, b, chain, roots + b * EPILOGUE_ROOTS[layer])
                    block_ended((layer + 1) * BLOCKS + b + 1)
                    assert chain.steps == EPILOGUE_STEPS[layer], (layer, chain.steps)
                steps += BLOCKS * EPILOGUE_STEPS[layer]
                roots += BLOCKS * EPILOGUE_ROOTS[layer]


def kernel(x, adj, L0_gnn_u, L1_gnn_W, L1_gnn_b, L2_gnn_W, L3_gnn_W):
    import numpy as np
    import concourse.bacc as bacc
    from concourse.bass_utils import run_bass_kernel_spmd

    a = np.asarray(adj).reshape(P, BLOCKS, BLOCK_TILES, P, TILES).transpose(1, 4, 3, 2, 0)
    stream = a[:, :SINGLE].reshape(BLOCKS, CHUNKS, CHUNK_TILES, P, COLS).transpose(0, 1, 3, 2, 4)
    cached = a[:, FIRST_CACHED:].reshape(BLOCKS, CACHED, P, COLS).transpose(0, 2, 1, 3)
    arrays = {
        "x_in": np.asarray(x).reshape(P, TILES * F),
        "stream_in": stream.reshape(BLOCKS, CHUNKS, P, CHUNK_TILES * COLS),
        "single_in": a[:, SINGLE].reshape(BLOCKS, P, COLS),
        "cached_in": cached.reshape(BLOCKS, P, CACHED * COLS),
        "u_in": np.asarray(L0_gnn_u).reshape(P, TILES * F),
        "w1_in": np.asarray(L1_gnn_W),
        "b1_in": np.asarray(L1_gnn_b).reshape(1, F),
        "w2_in": np.asarray(L2_gnn_W),
        "w3_in": np.asarray(L3_gnn_W).T,
    }
    arrays = {name: np.ascontiguousarray(v) for name, v in arrays.items()}
    nc = bacc.Bacc("TRN2", target_bir_lowering=False, num_devices=1)
    args = [nc.dram_tensor(name, v.shape, mybir.dt.from_np(v.dtype), kind="ExternalInput").ap()
            for name, v in arrays.items()]
    out = nc.dram_tensor("x_out", (P, TILES * F), mybir.dt.float32, kind="ExternalOutput").ap()
    gnn_stack(nc, *args, out)
    got = run_bass_kernel_spmd(nc, [arrays], core_ids=[0])
    return got.results[0]["x_out"].reshape(N, F)
```

```python
from contextlib import ExitStack

import concourse.bass as bass
from concourse import mybir

N = 8192
F = 64
P = 128
TILES = N // P
BLOCK_TILES = 8
BLOCKS = TILES // BLOCK_TILES
COLS = BLOCK_TILES * P
BANK = 512
BANKS = COLS // BANK
FEATS = BLOCK_TILES * F

CHUNK_TILES = 2
CHUNKS = 30
RING = 6
LOADS = CHUNKS // RING
SINGLE = CHUNKS * CHUNK_TILES
CACHED = TILES - SINGLE - 1
FIRST_CACHED = SINGLE + 1
MIDDLE = CHUNKS // 2

SOURCE_BLOCKS = (2, 3, 1, 4, 5, 6, 0, 7)
SOURCES = [B * BLOCK_TILES + t for B in SOURCE_BLOCKS for t in range(BLOCK_TILES)]
BLOCK_CHUNKS = BLOCK_TILES // CHUNK_TILES
FIRST_ORDER = list(range(CHUNKS))
LATER_ORDER = [(n + RING) % CHUNKS for n in range(CHUNKS)]
BOTH_SUMMED = 14
SUMMED_TILES = ([(0, 1) if c < BOTH_SUMMED else (0,) for c in range(CHUNKS)],
                [() if c < BOTH_SUMMED else (1,) for c in range(CHUNKS)])

LAYERS = 4
P_DROP = 0.1
LN_EPS = 1e-5
L2_EPS = 1e-12
LEAST_DEGREE = 2.0 ** -100

HAS_SELF = (False, True, True, False)
HAS_TOP = (False, True, False, True)
SUMS_DEGREE = (True, True, False, False)

FIRST_STEPS, PROLOGUE_STEPS, EPILOGUE_STEPS = 2, 8, (8, 19, 8, 3)
EPILOGUE_ROOTS = (1, 2, 1, 0)


PROLOGUE_AT = {0: (0, 1), 4: (2,), 8: (3,), 12: (4,), 16: (5,), 20: (6,), 24: (7,)}


def place_of(layer, n):
    return n if layer % 2 == 0 else n * -1 + (BLOCKS - 1)


def chunk_uses(layer, n, use):
    return layer * (BLOCKS * LOADS - 1) + 1 + n * LOADS + use


def gnn_stack(nc, x_in, stream_in, single_in, cached_in, u_in, w1_in, b1_in, w2_in, w3_in, x_out):
    fp32 = mybir.dt.float32
    ALU = mybir.AluOpType
    ACT = mybir.ActivationFunctionType
    X = mybir.AxisListType.X

    ctx = ExitStack()
    with ctx:
        def sbuf(name, shape):
            return ctx.enter_context(nc.sbuf_tensor(name, shape, fp32))

        def psum(name, shape):
            return ctx.enter_context(nc.psum_tensor(name, shape, fp32))

        def sem(name):
            return ctx.enter_context(nc.semaphore(name))

        x = sbuf("x", [P, TILES * F])
        h = [sbuf(f"h{i}", [P, TILES * F]) for i in range(2)]
        u = h[1]
        ring = [sbuf(f"ring{i}", [P, CHUNK_TILES * COLS]) for i in range(RING)]
        single = sbuf("single", [P, COLS])
        cache = sbuf("cache", [P, BLOCKS * CACHED * COLS])
        y_sb = sbuf("y_sb", [P, COLS])
        own_h = sbuf("own_h", [P, FEATS])
        own_hT = sbuf("own_hT", [P, COLS])
        row_sum = sbuf("row_sum", [P, COLS])
        ident = sbuf("ident", [P, P])
        ones = sbuf("ones", [P, 1])
        below = sbuf("below", [P, LAYERS, F])
        above = sbuf("above", [P, LAYERS, F])
        squares, z_sb = row_sum[:, 0:FEATS], row_sum[:, FEATS:2 * FEATS]
        early_squares, early_z = y_sb[:, 0:FEATS], y_sb[:, FEATS:2 * FEATS]
        mean = sbuf("mean", [P, BLOCK_TILES])
        to_root = sbuf("to_root", [P, 2 * BLOCK_TILES])
        rooted = sbuf("rooted", [P, 2 * BLOCK_TILES])
        inverse = sbuf("inverse", [P, 2 * BLOCK_TILES])
        inv_deg = sbuf("inv_deg", [P, BLOCK_TILES])
        degree = sbuf("degree", [P, TILES])
        deg_rsqrt = sbuf("deg_rsqrt", [P, TILES])

        Y = psum("Y", [P, COLS])
        HT = psum("HT", [P, COLS])
        Z = psum("Z", [P, FEATS])
        TOP = psum("TOP", [P, FEATS])
        DEG = psum("DEG", [P, BANK])

        x_loaded = [sem(f"x_loaded{i}") for i in range(4)]
        weights_loaded = sem("weights_loaded")
        weights_clear = sem("weights_clear")
        consts_ready = sem("consts_ready")
        chunk_loaded = [sem(f"chunk_loaded{i}") for i in range(RING)]
        single_loaded = sem("single_loaded")
        cache_loaded = sem("cache_loaded")
        chunk_multiplied = sem("chunk_multiplied")
        chunk_summed = sem("chunk_summed")
        half_summed = sem("half_summed")
        single_multiplied = sem("single_multiplied")
        rest_summed = sem("rest_summed")
        h_blocks = sem("h_blocks")
        own_h_ready = sem("own_h_ready")
        hT_done = sem("hT_done")
        hT_copied = sem("hT_copied")
        y_done = sem("y_done")
        y_copied = sem("y_copied")
        z_done = sem("z_done")
        root_asked = sem("root_asked")
        root_done = sem("root_done")
        dve_step = sem("dve_step")
        gp_step = sem("gp_step")
        out_stored = sem("out_stored")

        block = ctx.enter_context(nc.Block())

        def own(buf, b):
            return buf[:, bass.ds(b * FEATS, FEATS)]

        def by_tile(ap):
            return ap.rearrange("p (t f) -> p t f", f=F)

        def spread(ap):
            return ap.unsqueeze(2).to_broadcast([P, BLOCK_TILES, F])

        @block.sync
        def _(sp):
            def load_block(layer, n, b, first):
                blocks = layer * BLOCKS + n
                order = FIRST_ORDER if first else LATER_ORDER
                if first and 0 < layer <= 2:
                    sp.wait_ge(chunk_summed, layer * BLOCKS * CHUNKS + RING)
                    sp.wait_ge(rest_summed, 2 * layer * BLOCKS + 1)
                for i, c in enumerate(order):
                    if first and layer > 0 and i < RING:
                        continue
                    sp.wait_ge(chunk_multiplied, blocks * CHUNKS + i + 1)
                    if SUMS_DEGREE[layer] and (i < RING or SUMMED_TILES[layer][order[i - RING]]):
                        sp.wait_ge(chunk_summed, blocks * CHUNKS + i + 1)
                    sp.dma_start(ring[c % RING][:, :], stream_in[b, LATER_ORDER.index(c)]).then_inc(chunk_loaded[c % RING], 16)
                sp.wait_ge(single_multiplied, blocks + 1)
                if layer == 0:
                    sp.wait_ge(rest_summed, 2 * n + 1)
                sp.dma_start(single[:, :], single_in[b]).then_inc(single_loaded, 16)
                if layer == 0:
                    sp.dma_start(cache[:, bass.ds(b * CACHED * COLS, CACHED * COLS)],
                                 cached_in[b]).then_inc(cache_loaded, 16)

            for layer in range(LAYERS):
                load_block(layer, 0, place_of(layer, 0), True)
                with sp.Fori(1, BLOCKS) as n:
                    load_block(layer, n, sp.snap(place_of(layer, n)), False)

        @block.gpsimd
        def _(gp):
            nc.gpsimd.memset(above[:, :, :], 0.0).then_inc(weights_clear, 1)
            nc.gpsimd.memset(ident[:, :], 0.0)
            nc.gpsimd.memset(ones[:, :], 1.0)
            nc.gpsimd.memset(below[:, 0, :], 0.0).then_inc(gp_step, 1)
            gp.wait_ge(gp_step, 1)
            nc.gpsimd.affine_select(out=ident[:, :], in_=ident[:, :], compare_op=ALU.not_equal, fill=1.0,
                                    base=0, pattern=[[-1, P]], channel_multiplier=1)
            nc.gpsimd.affine_select(out=below[:, 0, :], in_=below[:, 0, :], compare_op=ALU.not_equal,
                                    fill=1.0, base=0, pattern=[[-1, F]],
                                    channel_multiplier=1).then_inc(gp_step, 1)
            gp.wait_ge(gp_step, 2)
            nc.gpsimd.affine_select(out=below[:, 0, :], in_=below[:, 0, :], compare_op=ALU.not_equal,
                                    fill=1.0, base=-F, pattern=[[-1, F]],
                                    channel_multiplier=1).then_inc(consts_ready, 1)

            for layer in range(1, LAYERS):
                gp.wait_ge(h_blocks, (layer + 1) * BLOCKS)
                with gp.Fori(0, BLOCKS) as n:
                    b = gp.snap(place_of(layer, n))
                    gp.wait_ge(y_done, (layer * BLOCKS + n) * BANKS)
                    nc.gpsimd.tensor_copy(own_h[:, :], own(h[layer % 2], b)).then_inc(own_h_ready, 1)
                    if layer == LAYERS - 1:
                        gp.wait_ge(h_blocks, (layer + 1) * BLOCKS + n + 1)
                        gp.dma_start(x_out[:, bass.ds(b * FEATS, FEATS)], own(x, b)).then_inc(out_stored, 16)
            gp.wait_ge(out_stored, 16 * BLOCKS)

        @block.scalar
        def _(act):
            quarter = TILES * F // 4
            for q in (1, 0, 2, 3):
                part = slice(q * quarter, (q + 1) * quarter)
                act.dma_start(x[:, part], x_in[:, part]).then_inc(x_loaded[q], 16)
                act.dma_start(u[:, part], u_in[:, part]).then_inc(x_loaded[q], 16)
            act.wait_ge(weights_clear, 1)
            act.dma_start(above[0:F, 1, :], w1_in[0:F, :]).then_inc(weights_loaded, 16)
            act.dma_start(above[F:F + 1, 1, :], b1_in).then_inc(weights_loaded, 16)
            act.dma_start(above[0:F, 3, :], w3_in[0:F, :]).then_inc(weights_loaded, 16)
            for half in (slice(0, F), slice(F, 2 * F)):
                act.dma_start(below[half, 1, :], w1_in[F:2 * F, :]).then_inc(weights_loaded, 16)
                act.dma_start(below[half, 2, :], w2_in).then_inc(weights_loaded, 16)
                act.dma_start(below[half, 3, :], w3_in[F:2 * F, :]).then_inc(weights_loaded, 16)

            def root(number):
                act.wait_ge(root_asked, number)
                nc.scalar.activation(rooted[:, :], to_root[:, :], ACT.Sqrt).then_inc(root_done, 1)

            with act.Fori(0, BLOCKS) as n:
                root(n + 1)
            roots, tops = BLOCKS, 0
            for layer in range(LAYERS):
                with act.Fori(0, BLOCKS) as b:
                    if HAS_TOP[layer]:
                        act.wait_ge(hT_done, tops + b + 1)
                        for k in range(BANKS):
                            cols = slice(k * BANK, (k + 1) * BANK)
                            nc.scalar.copy(own_hT[0:F, cols], HT[0:F, cols]).then_inc(hT_copied, 1)
                    for k in range(BANKS):
                        act.wait_ge(y_done, (layer * BLOCKS + b) * BANKS + k + 1)
                        cols = slice(k * BANK, (k + 1) * BANK)
                        nc.scalar.copy(y_sb[:, cols], Y[:, cols]).then_inc(y_copied, 1)
                    for r in range(EPILOGUE_ROOTS[layer]):
                        root(roots + b * EPILOGUE_ROOTS[layer] + r + 1)
                roots += BLOCKS * EPILOGUE_ROOTS[layer]
                tops += BLOCKS * HAS_TOP[layer]

        @block.tensor
        def _(pe):
            def multiply(h_now, tiles, first, last, place):
                done = []
                for k in range(BANKS):
                    for J, cols, half in tiles:
                        mm = nc.tensor.matmul(
                            Y[half * F:(half + 1) * F, k * BANK:(k + 1) * BANK],
                            h_now[:, J * F:(J + 1) * F], place(cols, k), start=first, stop=last)
                    done.append(mm)
                return done

            def fixed(buf, k):
                return buf[:, k * BANK:(k + 1) * BANK]

            def own_part(layer, tops, b):
                pe.wait_ge(own_h_ready, (layer - 1) * BLOCKS + b + 1)
                for t in range(BLOCK_TILES):
                    cols = slice(t * P, (t + 1) * P)
                    if HAS_SELF[layer]:
                        nc.tensor.matmul(Y[0:F, cols], own_h[:, t * F:(t + 1) * F], ident[:, :],
                                         start=False, stop=False)
                if HAS_TOP[layer]:
                    for t in range(BLOCK_TILES):
                        cols = slice(t * P, (t + 1) * P)
                        mm = nc.tensor.matmul(HT[0:F, cols], own_h[:, t * F:(t + 1) * F], ident[:, :],
                                              start=True, stop=True)
                    mm.then_inc(hT_done, 1)

            def one_block(layer, tops, n, b, first):
                h_now = h[layer % 2]
                blocks = layer * BLOCKS + n
                if first and layer > 0:
                    pe.wait_ge(h_blocks, (layer + 1) * BLOCKS - 1)
                for i, c in enumerate(FIRST_ORDER if first else LATER_ORDER):
                    at = c // BLOCK_CHUNKS
                    if first and c % BLOCK_CHUNKS == 0 and (layer == 0 or at == BLOCKS - 2):
                        pe.wait_ge(h_blocks, at + 1 if layer == 0 else (layer + 1) * BLOCKS)
                    if i == MIDDLE and (HAS_SELF[layer] or HAS_TOP[layer]):
                        own_part(layer, tops, n)
                    pe.wait_ge(chunk_loaded[c % RING], chunk_uses(layer, n, i // RING) * 16)
                    buf = ring[c % RING]
                    tiles = [(SOURCES[c * CHUNK_TILES + k], buf[:, k * COLS:(k + 1) * COLS], k)
                             for k in range(CHUNK_TILES)]
                    multiply(h_now, tiles, i == 0, False, fixed)[-1].then_inc(chunk_multiplied, 1)
                pe.wait_ge(single_loaded, (blocks + 1) * 16)
                multiply(h_now, [(SOURCES[SINGLE], single, 1)], False, True,
                         fixed)[-1].then_inc(single_multiplied, 1)
                if layer == 0:
                    pe.wait_ge(cache_loaded, (n + 1) * 16)
                for m in range(CACHED):
                    def kept(_, k):
                        return cache[:, bass.ds((b * CACHED + m) * COLS + k * BANK, BANK)]
                    done = multiply(h_now, [(SOURCES[FIRST_CACHED + m], cache, 0)], False, m == CACHED - 1, kept)
                for mm in done:
                    mm.then_inc(y_done, 1)

                pe.wait_ge(h_blocks, blocks + BLOCKS)
                if SUMS_DEGREE[layer]:
                    pe.wait_ge(rest_summed, 2 * blocks + 3)
                    for t in range(BLOCK_TILES):
                        nc.tensor.matmul(DEG[:, t:t + 1], row_sum[:, t * P:(t + 1) * P], ones[:, :],
                                         start=True, stop=True)
                if HAS_TOP[layer]:
                    pe.wait_ge(hT_copied, (tops + n + 1) * BANKS)
                    for t in range(BLOCK_TILES):
                        nc.tensor.matmul(TOP[:, t * F:(t + 1) * F], own_hT[:, t * P:(t + 1) * P],
                                         above[:, layer, :], start=True, stop=True)
                for t in range(BLOCK_TILES):
                    if t * P % BANK == 0:
                        pe.wait_ge(y_copied, blocks * BANKS + t * P // BANK + 1)
                    mm = nc.tensor.matmul(Z[:, t * F:(t + 1) * F], y_sb[:, t * P:(t + 1) * P],
                                          below[:, layer, :], start=True, stop=True)
                mm.then_inc(z_done, 1)

            pe.wait_ge(consts_ready, 2)
            tops = 0
            for layer in range(LAYERS):
                if layer == 1:
                    pe.wait_ge(weights_loaded, 9 * 16)
                one_block(layer, tops, 0, place_of(layer, 0), True)
                with pe.Fori(1, BLOCKS) as n:
                    one_block(layer, tops, n, pe.snap(place_of(layer, n)), False)
                tops += BLOCKS * HAS_TOP[layer]

        @block.vector
        def _(dve):
            nc.vector.memset(mean[:, 0:1], 0.0).then_inc(chunk_multiplied, RING)
            nc.vector.memset(mean[:, 1:2], 0.0).then_inc(chunk_summed, RING)
            nc.vector.memset(mean[:, 2:3], 0.0).then_inc(single_multiplied, 1)
            nc.vector.memset(mean[:, 3:4], 0.0).then_inc(rest_summed, 1)
            nc.vector.memset(to_root[:, :], 1.0).then_inc(dve_step, 1)
            nc.vector.memset(own_hT[:, :], 0.0).then_inc(dve_step, 1)
            dve.wait_ge(dve_step, FIRST_STEPS)
            nc.vector.memset(own_hT[F:F + 1, :], 1.0).then_inc(consts_ready, 1)

            class Chain:

                def __init__(self, before):
                    self.before, self.steps = before, 0

                def __call__(self, instruction):
                    self.steps += 1
                    instruction.then_inc(dve_step, 1)
                    dve.wait_ge(dve_step, self.before + self.steps)

            def ask_roots(chain, roots):
                dve.wait_ge(root_done, roots)

            def add(chain, out, a, c):
                chain(nc.vector.tensor_tensor(out, a, c, ALU.add))

            def copy(chain, out, a):
                chain(nc.vector.tensor_scalar(out, a, 1.0, None, ALU.mult))

            def new_state(chain, xs, z):
                add(chain, z_sb, z, xs)
                copy(chain, xs, z_sb)

            def layer_norm(chain, hs, roots, scale=None, last=None, scratch=(z_sb, squares)):
                z, sq = scratch
                c3, s3 = by_tile(z), by_tile(sq)
                first = slice(0, BLOCK_TILES)
                chain(nc.vector.tensor_reduce(mean[:, :], c3, X, ALU.add))
                chain(nc.vector.scalar_tensor_tensor(out=c3, in0=spread(mean[:, :]), scalar=-1.0 / F, in1=c3,
                                                     op0=ALU.mult, op1=ALU.add))
                chain(nc.vector.tensor_tensor(sq, z, z, ALU.mult))
                chain(nc.vector.tensor_reduce(inverse[:, first], s3, X, ALU.add))
                nc.vector.tensor_scalar(to_root[:, first], inverse[:, first], 1.0 / F, LN_EPS, ALU.mult,
                                        ALU.add).then_inc(root_asked, 1)
                dve.wait_ge(root_done, roots)
                chain(nc.vector.reciprocal(inverse[:, first], rooted[:, first]))
                if scale is not None:
                    chain(scale(inverse[:, first]))
                done = nc.vector.scalar_tensor_tensor(out=by_tile(hs), in0=c3, scalar=0.0,
                                                      in1=spread(inverse[:, first]), op0=ALU.max, op1=ALU.mult)
                if last is None:
                    done.then_inc(h_blocks, 1)
                else:
                    chain(done)
                    last().then_inc(h_blocks, 1)

            def block_ended(count):
                dve.wait_ge(h_blocks, count)

            def prologue(n, chain):
                b = SOURCE_BLOCKS[n]
                dve.wait_ge(x_loaded[b // 2], 32)
                chain(nc.vector.tensor_copy(early_z, own(x, b)))
                layer_norm(chain, own(h[0], b), n + 1, scratch=(early_z, early_squares),
                           scale=lambda r: nc.vector.tensor_scalar(r, r, 1.0 / (1.0 - P_DROP), None, ALU.mult),
                           last=lambda: nc.vector.scalar_tensor_tensor(
                               out=own(h[0], b), in0=own(u, b), scalar=P_DROP, in1=own(h[0], b),
                               op0=ALU.is_ge, op1=ALU.mult))
                block_ended(n + 1)

            def sum_chunk(layer, n, i, c, before, after, halves):
                start = (layer * BLOCKS + n) * CHUNKS + RING
                dve.wait_ge(chunk_loaded[c % RING], chunk_uses(layer, n, i // RING) * 16)
                tiles = [ring[c % RING][:, k * COLS:(k + 1) * COLS] for k in SUMMED_TILES[layer][c]]
                if before == 0:
                    step = (nc.vector.tensor_tensor(row_sum[:, :], tiles[0], tiles[1], ALU.add)
                            if len(tiles) == 2 else nc.vector.tensor_copy(row_sum[:, :], tiles[0]))
                else:
                    dve.wait_ge(chunk_summed, start + before)
                    step = nc.vector.tensor_tensor(row_sum[:, :], row_sum[:, :], tiles[0], ALU.add)
                    if len(tiles) == 2:
                        step.then_inc(half_summed, 1)
                        dve.wait_ge(half_summed, n * (BOTH_SUMMED - 1) + halves + 1)
                        step = nc.vector.tensor_tensor(row_sum[:, :], row_sum[:, :], tiles[1], ALU.add)
                step.then_inc(chunk_summed, after - before)

            def sum_rest(layer, n, b):
                blocks = layer * BLOCKS + n
                dve.wait_ge(chunk_summed, (blocks + 1) * CHUNKS + RING)
                if layer == 0:
                    dve.wait_ge(single_loaded, (n + 1) * 16)
                    dve.wait_ge(cache_loaded, (n + 1) * 16)
                kept = [cache[:, bass.ds((b * CACHED + m) * COLS, COLS)] for m in range(CACHED)]
                for m, tile in enumerate([single[:, :], kept[0]] if layer == 0 else kept[1:]):
                    if m:
                        dve.wait_ge(rest_summed, 2 * blocks + m + 1)
                    nc.vector.tensor_tensor(row_sum[:, :], row_sum[:, :], tile, ALU.add).then_inc(rest_summed, 1)

            def sum_tiles(layer, n, b, first):
                order = FIRST_ORDER if first else LATER_ORDER
                last = max(i for i, c in enumerate(order) if SUMMED_TILES[layer][c])
                before = halves = 0
                for i, c in enumerate(order):
                    if layer == 0 and first and i in PROLOGUE_AT:
                        for k in PROLOGUE_AT[i]:
                            prologue(k, Chain(FIRST_STEPS + k * PROLOGUE_STEPS))
                    if SUMMED_TILES[layer][c]:
                        after = CHUNKS if i == last else i + 1
                        sum_chunk(layer, n, i, c, before, after, halves)
                        halves += before > 0 and len(SUMMED_TILES[layer][c]) == 2
                        before = after
                sum_rest(layer, n, b)

            def epilogue(layer, n, b, chain, roots):
                blocks = layer * BLOCKS + n
                xs, hs = own(x, b), own(h[(layer + 1) % 2], b)
                z, z3, Z3, s3 = z_sb, by_tile(z_sb), by_tile(Z[:, :]), by_tile(squares)
                deg, rsq = (a[:, bass.ds(b * BLOCK_TILES, BLOCK_TILES)] for a in (degree, deg_rsqrt))
                lo, hi = slice(0, BLOCK_TILES), slice(BLOCK_TILES, 2 * BLOCK_TILES)
                dve.wait_ge(z_done, blocks + 1)
                if layer == 0:
                    copy(chain, deg, DEG[:, lo])
                    new_state(chain, xs, Z[:, :])
                    layer_norm(chain, hs, roots + 1)
                elif layer == 1:
                    chain(nc.vector.scalar_tensor_tensor(out=deg, in0=DEG[:, lo], scalar=1.0, in1=deg,
                                                         op0=ALU.add, op1=ALU.add))
                    chain(nc.vector.tensor_scalar(inv_deg[:, :], deg, 1.0, None, ALU.max))
                    chain(nc.vector.reciprocal(inv_deg[:, :], inv_deg[:, :]))
                    chain(nc.vector.tensor_tensor(z3, Z3, spread(inv_deg[:, :]), ALU.mult))
                    add(chain, z, TOP[:, :], z)
                    chain(nc.vector.scalar_tensor_tensor(out=squares, in0=z, scalar=0.0, in1=z,
                                                         op0=ALU.max, op1=ALU.mult))
                    chain(nc.vector.tensor_reduce(mean[:, :], s3, X, ALU.add))
                    chain(nc.vector.tensor_scalar(to_root[:, lo], mean[:, :], L2_EPS ** 2, None, ALU.max))
                    nc.vector.tensor_scalar(to_root[:, hi], deg, LEAST_DEGREE, None,
                                            ALU.max).then_inc(root_asked, 1)
                    dve.wait_ge(root_done, roots + 1)
                    chain(nc.vector.reciprocal(inverse[:, :], rooted[:, :]))
                    chain(nc.vector.scalar_tensor_tensor(out=rsq, in0=deg, scalar=0.0, in1=inverse[:, hi],
                                                         op0=ALU.is_gt, op1=ALU.mult))
                    chain(nc.vector.scalar_tensor_tensor(out=z3, in0=z3, scalar=0.0,
                                                         in1=spread(inverse[:, lo]), op0=ALU.max, op1=ALU.mult))
                    new_state(chain, xs, z)
                    layer_norm(chain, hs, roots + 2,
                               scale=lambda r: nc.vector.tensor_tensor(r, r, rsq, ALU.mult))
                elif layer == 2:
                    chain(nc.vector.tensor_tensor(z3, Z3, spread(rsq), ALU.mult))
                    new_state(chain, xs, z)
                    layer_norm(chain, hs, roots + 1)
                else:
                    chain(nc.vector.reciprocal(inv_deg[:, :], deg))
                    chain(nc.vector.tensor_tensor(z3, Z3, spread(inv_deg[:, :]), ALU.mult))
                    add(chain, z, TOP[:, :], z)
                    nc.vector.tensor_tensor(xs, z, xs, ALU.add).then_inc(h_blocks, 1)

            def one_block(layer, n, b, first, steps, roots):
                if SUMS_DEGREE[layer]:
                    sum_tiles(layer, n, b, first)
                chain = Chain(steps + n * EPILOGUE_STEPS[layer])
                epilogue(layer, n, b, chain, roots + n * EPILOGUE_ROOTS[layer])
                block_ended((layer + 1) * BLOCKS + n + 1)
                assert chain.steps == EPILOGUE_STEPS[layer], (layer, chain.steps)

            steps, roots = FIRST_STEPS + BLOCKS * PROLOGUE_STEPS, BLOCKS
            for layer in range(LAYERS):
                one_block(layer, 0, place_of(layer, 0), True, steps, roots)
                with dve.Fori(1, BLOCKS) as n:
                    one_block(layer, n, dve.snap(place_of(layer, n)), False, steps, roots)
                steps += BLOCKS * EPILOGUE_STEPS[layer]
                roots += BLOCKS * EPILOGUE_ROOTS[layer]


def kernel(x, adj, L0_gnn_u, L1_gnn_W, L1_gnn_b, L2_gnn_W, L3_gnn_W):
    import numpy as np
    import concourse.bacc as bacc
    from concourse.bass_utils import run_bass_kernel_spmd

    a = np.asarray(adj).reshape(P, BLOCKS, BLOCK_TILES, P, TILES).transpose(1, 4, 3, 2, 0)
    a = a[:, SOURCES]
    stream = a[:, :SINGLE].reshape(BLOCKS, CHUNKS, CHUNK_TILES, P, COLS).transpose(0, 1, 3, 2, 4)
    stream = stream[:, LATER_ORDER]
    cached = a[:, FIRST_CACHED:].reshape(BLOCKS, CACHED, P, COLS).transpose(0, 2, 1, 3)
    arrays = {
        "x_in": np.asarray(x).reshape(P, TILES * F),
        "stream_in": stream.reshape(BLOCKS, CHUNKS, P, CHUNK_TILES * COLS),
        "single_in": a[:, SINGLE].reshape(BLOCKS, P, COLS),
        "cached_in": cached.reshape(BLOCKS, P, CACHED * COLS),
        "u_in": np.asarray(L0_gnn_u).reshape(P, TILES * F),
        "w1_in": np.asarray(L1_gnn_W),
        "b1_in": np.asarray(L1_gnn_b).reshape(1, F),
        "w2_in": np.asarray(L2_gnn_W),
        "w3_in": np.asarray(L3_gnn_W).T,
    }
    arrays = {name: np.ascontiguousarray(v) for name, v in arrays.items()}
    nc = bacc.Bacc("TRN2", target_bir_lowering=False, num_devices=1, dynamic_dma_scratch_size=2048)
    args = [nc.dram_tensor(name, v.shape, mybir.dt.from_np(v.dtype), kind="ExternalInput").ap()
            for name, v in arrays.items()]
    out = nc.dram_tensor("x_out", (P, TILES * F), mybir.dt.float32, kind="ExternalOutput").ap()
    gnn_stack(nc, *args, out)
    got = run_bass_kernel_spmd(nc, [arrays], core_ids=[0])
    return got.results[0]["x_out"].reshape(N, F)
```

```python
from contextlib import ExitStack

import concourse.bass as bass
from concourse import mybir

N = 8192
F = 64
P = 128
TILES = N // P
BLOCK_TILES = 8
BLOCKS = TILES // BLOCK_TILES
COLS = BLOCK_TILES * P
BANK = 512
BANKS = COLS // BANK
FEATS = BLOCK_TILES * F

CHUNK_TILES = 3
CHUNKS = 20
RING = 5
LOADS = CHUNKS // RING
PAIRS = CHUNKS * CHUNK_TILES // 2
CACHED = TILES - CHUNKS * CHUNK_TILES - 1
MIDDLE = CHUNKS // 2
MIDDLE_PAIR = PAIRS // 2
TOP_PAIR = MIDDLE_PAIR + 3
FINISH_PAIR, FIRST_FINISH_PAIR = 1, 5

SOURCE_BLOCKS = (2, 3, 1, 4, 5, 6, 0, 7)
SOURCES = [B * BLOCK_TILES + t for B in SOURCE_BLOCKS for t in range(BLOCK_TILES)]
APART = slice(2 * BLOCK_TILES - 1 - CACHED, 2 * BLOCK_TILES)
SINGLE, *KEPT = SOURCES[APART]
del SOURCES[APART]
BLOCK_AT = {next(i for i, J in enumerate(SOURCES) if J // BLOCK_TILES == B) // CHUNK_TILES: rank
            for rank, B in enumerate(SOURCE_BLOCKS)}
FIRST_ORDER = list(range(CHUNKS))
LATER_ORDER = [(n + RING) % CHUNKS for n in range(CHUNKS)]
WHOLLY_FIRST = CHUNKS // 2
SUMMED_TILES = ([(0, 1, 2) if c < WHOLLY_FIRST else (0,) for c in range(CHUNKS)],
                [() if c < WHOLLY_FIRST else (1, 2) for c in range(CHUNKS)])
PARTS = tuple(sum(map(len, tiles)) - 1 - sum(map(bool, tiles)) for tiles in SUMMED_TILES)
REST_AT = MIDDLE + 1

LAYERS = 4
P_DROP = 0.1
LN_EPS = 1e-5
L2_EPS = 1e-12
LEAST_DEGREE = 2.0 ** -100

HAS_SELF = (False, True, True, False)
HAS_TOP = (False, True, False, True)
SUMS_DEGREE = (True, True, False, False)

FIRST_STEPS, PROLOGUE_STEPS, EPILOGUE_STEPS = 1, 8, (8, 20, 8, 3)
EPILOGUE_ROOTS = (1, 2, 1, 0)

PROLOGUE_AT = {0: (0, 1), 2: (2,), 4: (3,), 7: (4,), 10: (5,), 12: (6,), 15: (7,)}


def place_of(layer, n):
    return n if layer % 2 == 0 else n * -1 + (BLOCKS - 1)


def tops_before(layer):
    return BLOCKS * sum(HAS_TOP[:layer])


def chunk_uses(layer, n, use):
    return layer * (BLOCKS * LOADS - 1) + 1 + n * LOADS + use


def gnn_stack(nc, x_in, stream_in, single_in, cached_in, u_in, w1_in, b1_in, w2_in, w3_in, x_out):
    fp32 = mybir.dt.float32
    ALU = mybir.AluOpType
    ACT = mybir.ActivationFunctionType
    X = mybir.AxisListType.X

    ctx = ExitStack()
    with ctx:
        def sbuf(name, shape):
            return ctx.enter_context(nc.sbuf_tensor(name, shape, fp32))

        def psum(name, shape):
            return ctx.enter_context(nc.psum_tensor(name, shape, fp32))

        def sem(name):
            return ctx.enter_context(nc.semaphore(name))

        x = sbuf("x", [P, TILES * F])
        h = [sbuf(f"h{i}", [P, TILES * F]) for i in range(2)]
        u = h[1]
        ring = [sbuf(f"ring{i}", [P, CHUNK_TILES * COLS]) for i in range(RING)]
        single = sbuf("single", [P, COLS])
        cache = sbuf("cache", [P, BLOCKS * CACHED * COLS])
        y_sb = sbuf("y_sb", [P, COLS])
        own_h = sbuf("own_h", [P, FEATS])
        own_hT = y_sb[0:F, :]
        row_sum = sbuf("row_sum", [P, COLS])
        ident = sbuf("ident", [P, P])
        ones = sbuf("ones", [P, 1])
        below = sbuf("below", [P, LAYERS, F])
        above = sbuf("above", [F, LAYERS, F])
        bias = sbuf("bias", [P, F])
        squares, z_sb = row_sum[:, 0:FEATS], row_sum[:, FEATS:2 * FEATS]
        early_squares, early_z = y_sb[:, 0:FEATS], y_sb[:, FEATS:2 * FEATS]
        mean = sbuf("mean", [P, BLOCK_TILES])
        to_root = sbuf("to_root", [P, 2 * BLOCK_TILES])
        rooted = sbuf("rooted", [P, 2 * BLOCK_TILES])
        inverse = sbuf("inverse", [P, 2 * BLOCK_TILES])
        inv_deg = sbuf("inv_deg", [P, BLOCK_TILES])
        degree = sbuf("degree", [P, TILES])
        deg_rsqrt = sbuf("deg_rsqrt", [P, TILES])

        Y = psum("Y", [P, COLS])
        HT = psum("HT", [P, COLS])
        Z = psum("Z", [P, FEATS])
        TOP = psum("TOP", [P, FEATS])
        DEG = psum("DEG", [P, BANK])

        x_loaded = [sem(f"x_loaded{i}") for i in range(4)]
        weights_loaded = sem("weights_loaded")
        consts_ready = sem("consts_ready")
        chunk_loaded = [sem(f"chunk_loaded{i}") for i in range(RING)]
        single_loaded = sem("single_loaded")
        cache_loaded = sem("cache_loaded")
        chunk_multiplied = sem("chunk_multiplied")
        chunk_summed = sem("chunk_summed")
        part_summed = sem("part_summed")
        single_multiplied = sem("single_multiplied")
        rest_summed = sem("rest_summed")
        h_blocks = sem("h_blocks")
        own_h_ready = sem("own_h_ready")
        hT_done = sem("hT_done")
        hT_copied = sem("hT_copied")
        first_bank_done = sem("first_bank_done")
        y_copied = sem("y_copied")
        z_done = sem("z_done")
        root_asked = sem("root_asked")
        root_done = sem("root_done")
        dve_step = sem("dve_step")
        gp_step = sem("gp_step")
        out_stored = sem("out_stored")

        block = ctx.enter_context(nc.Block())

        def own(buf, b):
            return buf[:, bass.ds(b * FEATS, FEATS)]

        def by_tile(ap):
            return ap.rearrange("p (t f) -> p t f", f=F)

        def spread(ap):
            return ap.unsqueeze(2).to_broadcast([P, BLOCK_TILES, F])

        @block.sync
        def _(sp):
            def load_block(layer, n, b, first):
                blocks = layer * BLOCKS + n
                order = FIRST_ORDER if first else LATER_ORDER
                if first and 0 < layer <= 2:
                    sp.wait_ge(chunk_summed, layer * BLOCKS * CHUNKS + RING)
                    sp.wait_ge(rest_summed, 2 * layer * BLOCKS + 1)
                for i, c in enumerate(order):
                    if i == MIDDLE and not (first and layer > 0):
                        sp.wait_ge(single_multiplied, blocks + 1)
                        if layer == 0:
                            sp.wait_ge(rest_summed, 2 * n + 1)
                        sp.dma_start(single[:, :], single_in[b]).then_inc(single_loaded, 16)
                        if layer == 0:
                            sp.dma_start(cache[:, bass.ds(b * CACHED * COLS, CACHED * COLS)],
                                         cached_in[b]).then_inc(cache_loaded, 16)
                    if first and layer > 0 and i < RING:
                        continue
                    sp.wait_ge(chunk_multiplied, blocks * CHUNKS + i + 1)
                    if SUMS_DEGREE[layer] and (i < RING or SUMMED_TILES[layer][order[i - RING]]):
                        sp.wait_ge(chunk_summed, blocks * CHUNKS + i + 1)
                    sp.dma_start(ring[c % RING][:, :],
                                 stream_in[b, LATER_ORDER.index(c)]).then_inc(chunk_loaded[c % RING], 16)

            for layer in range(LAYERS):
                load_block(layer, 0, place_of(layer, 0), True)
                with sp.Fori(1, BLOCKS) as n:
                    load_block(layer, n, sp.snap(place_of(layer, n)), False)

        @block.gpsimd
        def _(gp):
            nc.gpsimd.memset(ident[:, :], 0.0)
            nc.gpsimd.memset(ones[:, :], 1.0)
            nc.gpsimd.memset(below[:, 0, :], 0.0).then_inc(gp_step, 1)
            gp.wait_ge(gp_step, 1)
            nc.gpsimd.affine_select(out=ident[:, :], in_=ident[:, :], compare_op=ALU.not_equal, fill=1.0,
                                    base=0, pattern=[[-1, P]], channel_multiplier=1)
            nc.gpsimd.affine_select(out=below[:, 0, :], in_=below[:, 0, :], compare_op=ALU.not_equal,
                                    fill=1.0, base=0, pattern=[[-1, F]],
                                    channel_multiplier=1).then_inc(gp_step, 1)
            gp.wait_ge(gp_step, 2)
            nc.gpsimd.affine_select(out=below[:, 0, :], in_=below[:, 0, :], compare_op=ALU.not_equal,
                                    fill=1.0, base=-F, pattern=[[-1, F]],
                                    channel_multiplier=1).then_inc(consts_ready, 1)

            for layer in range(1, LAYERS):
                gp.wait_ge(h_blocks, (layer + 1) * BLOCKS)
                with gp.Fori(0, BLOCKS) as n:
                    b = gp.snap(place_of(layer, n))
                    gp.wait_ge(chunk_multiplied, (layer * BLOCKS + n) * CHUNKS + RING)
                    nc.gpsimd.tensor_copy(own_h[:, :], own(h[layer % 2], b)).then_inc(own_h_ready, 1)
                    if layer == LAYERS - 1:
                        gp.wait_ge(h_blocks, (layer + 1) * BLOCKS + n + 1)
                        gp.dma_start(x_out[:, bass.ds(b * FEATS, FEATS)], own(x, b)).then_inc(out_stored, 16)
            gp.wait_ge(out_stored, 16 * BLOCKS)

        @block.scalar
        def _(act):
            quarter = TILES * F // 4
            for q in (1, 0, 2, 3):
                part = slice(q * quarter, (q + 1) * quarter)
                act.dma_start(x[:, part], x_in[:, part]).then_inc(x_loaded[q], 16)
                act.dma_start(u[:, part], u_in[:, part]).then_inc(x_loaded[q], 16)
            act.dma_start(above[0:F, 1, :], w1_in[0:F, :]).then_inc(weights_loaded, 16)
            act.dma_start(bias[:, :], b1_in.to_broadcast([P, F])).then_inc(weights_loaded, 16)
            act.dma_start(above[0:F, 3, :], w3_in[0:F, :]).then_inc(weights_loaded, 16)
            for half in (slice(0, F), slice(F, 2 * F)):
                act.dma_start(below[half, 1, :], w1_in[F:2 * F, :]).then_inc(weights_loaded, 16)
                act.dma_start(below[half, 2, :], w2_in).then_inc(weights_loaded, 16)
                act.dma_start(below[half, 3, :], w3_in[F:2 * F, :]).then_inc(weights_loaded, 16)

            def root(number):
                act.wait_ge(root_asked, number)
                nc.scalar.activation(rooted[:, :], to_root[:, :], ACT.Sqrt).then_inc(root_done, 1)

            with act.Fori(0, BLOCKS) as n:
                root(n + 1)
            roots = BLOCKS
            for layer in range(LAYERS):
                with act.Fori(0, BLOCKS) as b:
                    if HAS_TOP[layer]:
                        act.wait_ge(hT_done, tops_before(layer) + b + 1)
                        for k in range(BANKS):
                            cols = slice(k * BANK, (k + 1) * BANK)
                            nc.scalar.copy(own_hT[:, cols], HT[0:F, cols]).then_inc(hT_copied, 1)
                    for k in range(BANKS):
                        if k < BANKS - 1:
                            act.wait_ge(first_bank_done, layer * BLOCKS + b + 1)
                        else:
                            act.wait_ge(chunk_multiplied, (layer * BLOCKS + b + 1) * CHUNKS + RING)
                        cols = slice(k * BANK, (k + 1) * BANK)
                        nc.scalar.copy(y_sb[:, cols], Y[:, cols]).then_inc(y_copied, 1)
                    for r in range(EPILOGUE_ROOTS[layer]):
                        root(roots + b * EPILOGUE_ROOTS[layer] + r + 1)
                roots += BLOCKS * EPILOGUE_ROOTS[layer]

        @block.tensor
        def _(pe):
            def multiply(h_now, tiles, first, last, place):
                done = []
                for k in range(BANKS):
                    for J, cols, half in tiles:
                        mm = nc.tensor.matmul(
                            Y[half * F:(half + 1) * F, k * BANK:(k + 1) * BANK],
                            h_now[:, J * F:(J + 1) * F], place(cols, k), start=first, stop=last)
                    done.append(mm)
                return done

            def fixed(buf, k):
                return buf[:, k * BANK:(k + 1) * BANK]

            def own_part(layer, n):
                pe.wait_ge(own_h_ready, (layer - 1) * BLOCKS + n + 1)
                for t in range(BLOCK_TILES):
                    cols = slice(t * P, (t + 1) * P)
                    if HAS_SELF[layer]:
                        nc.tensor.matmul(Y[0:F, cols], own_h[:, t * F:(t + 1) * F], ident[:, :],
                                         start=False, stop=False)
                if HAS_TOP[layer]:
                    for t in range(BLOCK_TILES):
                        cols = slice(t * P, (t + 1) * P)
                        mm = nc.tensor.matmul(HT[0:F, cols], own_h[:, t * F:(t + 1) * F], ident[:, :],
                                              start=True, stop=True)
                    mm.then_inc(hT_done, 1)

            def finish(layer, n):
                blocks = layer * BLOCKS + n
                pe.wait_ge(h_blocks, blocks + BLOCKS)
                if SUMS_DEGREE[layer]:
                    pe.wait_ge(chunk_summed, (blocks + 1) * CHUNKS + RING)
                    for t in range(BLOCK_TILES):
                        nc.tensor.matmul(DEG[:, t:t + 1], row_sum[:, t * P:(t + 1) * P], ones[:, :],
                                         start=True, stop=True)
                pe.wait_ge(y_copied, (blocks + 1) * BANKS)
                for t in range(BLOCK_TILES):
                    mm = nc.tensor.matmul(Z[:, t * F:(t + 1) * F], y_sb[:, t * P:(t + 1) * P],
                                          below[:, layer, :], start=True, stop=True)
                mm.then_inc(z_done, 1)

            def apart(layer, n, b):
                h_now = h[layer % 2]
                pe.wait_ge(single_loaded, (layer * (BLOCKS - 1) + n + 1) * 16)
                multiply(h_now, [(SINGLE, single, 1)], False, False, fixed)[-1].then_inc(single_multiplied, 1)
                if layer == 0:
                    pe.wait_ge(cache_loaded, (n + 1) * 16)
                for m, J in enumerate(KEPT):
                    def kept(_, k):
                        return cache[:, bass.ds((b * CACHED + m) * COLS + k * BANK, BANK)]
                    multiply(h_now, [(J, cache, 0)], False, False, kept)
                if HAS_SELF[layer] or HAS_TOP[layer]:
                    own_part(layer, n)

            def top(layer, n):
                pe.wait_ge(h_blocks, (layer + 1) * BLOCKS + n)
                pe.wait_ge(hT_copied, (tops_before(layer) + n + 1) * BANKS)
                for t in range(BLOCK_TILES):
                    nc.tensor.matmul(TOP[:, t * F:(t + 1) * F], own_hT[:, t * P:(t + 1) * P],
                                     above[:, layer, :], start=True, stop=True)

            def one_block(layer, n, b, first):
                h_now = h[layer % 2]
                blocks = layer * BLOCKS + n
                if not (first and layer == 0):
                    pe.wait_ge(y_copied, blocks * BANKS)
                if first and layer > 0:
                    pe.wait_ge(h_blocks, (layer + 1) * BLOCKS - 1)
                order = FIRST_ORDER if first else LATER_ORDER
                for pair in range(PAIRS):
                    if pair == FINISH_PAIR and not first:
                        finish(layer, n - 1)
                    elif pair == FIRST_FINISH_PAIR and first and layer > 0:
                        finish(layer - 1, BLOCKS - 1)
                    if pair == MIDDLE_PAIR:
                        apart(layer, n, b)
                    if pair == TOP_PAIR and HAS_TOP[layer]:
                        top(layer, n)
                    tiles, ended = [], False
                    for half in range(2):
                        i, k = divmod(2 * pair + half, CHUNK_TILES)
                        c = order[i]
                        if k == 0:
                            rank = BLOCK_AT.get(c)
                            if first and layer == 0 and rank is not None:
                                pe.wait_ge(h_blocks, rank + 1)
                            elif first and rank == BLOCKS - 2:
                                pe.wait_ge(h_blocks, (layer + 1) * BLOCKS)
                            pe.wait_ge(chunk_loaded[c % RING], chunk_uses(layer, n, i // RING) * 16)
                        ended = ended or k == CHUNK_TILES - 1
                        tiles.append((SOURCES[c * CHUNK_TILES + k],
                                      ring[c % RING][:, k * COLS:(k + 1) * COLS], half))
                    done = multiply(h_now, tiles, pair == 0, pair == PAIRS - 1, fixed)
                    if ended:
                        done[-1].then_inc(chunk_multiplied, 1)
                done[0].then_inc(first_bank_done, 1)

            pe.wait_ge(consts_ready, 1)
            for layer in range(LAYERS):
                if layer == 1:
                    pe.wait_ge(weights_loaded, 9 * 16)
                one_block(layer, 0, place_of(layer, 0), True)
                with pe.Fori(1, BLOCKS) as n:
                    one_block(layer, n, pe.snap(place_of(layer, n)), False)
            finish(LAYERS - 1, BLOCKS - 1)

        @block.vector
        def _(dve):
            nc.vector.memset(mean[:, 0:1], 0.0).then_inc(chunk_multiplied, RING)
            nc.vector.memset(mean[:, 1:2], 0.0).then_inc(chunk_summed, RING)
            nc.vector.memset(mean[:, 2:3], 0.0).then_inc(single_multiplied, 1)
            nc.vector.memset(mean[:, 3:4], 0.0).then_inc(rest_summed, 1)
            nc.vector.memset(to_root[:, :], 1.0).then_inc(dve_step, 1)
            dve.wait_ge(dve_step, FIRST_STEPS)

            class Chain:

                def __init__(self, before):
                    self.before, self.steps = before, 0

                def __call__(self, instruction):
                    self.steps += 1
                    instruction.then_inc(dve_step, 1)
                    dve.wait_ge(dve_step, self.before + self.steps)

            def add(chain, out, a, c):
                chain(nc.vector.tensor_tensor(out, a, c, ALU.add))

            def copy(chain, out, a):
                chain(nc.vector.tensor_scalar(out, a, 1.0, None, ALU.mult))

            def new_state(chain, xs, z):
                add(chain, z_sb, z, xs)
                copy(chain, xs, z_sb)

            def layer_norm(chain, hs, roots, scale=None, last=None, scratch=(z_sb, squares)):
                z, sq = scratch
                c3, s3 = by_tile(z), by_tile(sq)
                first = slice(0, BLOCK_TILES)
                chain(nc.vector.tensor_reduce(mean[:, :], c3, X, ALU.add))
                chain(nc.vector.scalar_tensor_tensor(out=c3, in0=spread(mean[:, :]), scalar=-1.0 / F, in1=c3,
                                                     op0=ALU.mult, op1=ALU.add))
                chain(nc.vector.tensor_tensor(sq, z, z, ALU.mult))
                chain(nc.vector.tensor_reduce(inverse[:, first], s3, X, ALU.add))
                nc.vector.tensor_scalar(to_root[:, first], inverse[:, first], 1.0 / F, LN_EPS, ALU.mult,
                                        ALU.add).then_inc(root_asked, 1)
                dve.wait_ge(root_done, roots)
                chain(nc.vector.reciprocal(inverse[:, first], rooted[:, first]))
                if scale is not None:
                    chain(scale(inverse[:, first]))
                done = nc.vector.scalar_tensor_tensor(out=by_tile(hs), in0=c3, scalar=0.0,
                                                      in1=spread(inverse[:, first]), op0=ALU.max, op1=ALU.mult)
                if last is None:
                    done.then_inc(h_blocks, 1)
                else:
                    chain(done)
                    last().then_inc(h_blocks, 1)

            def block_ended(count):
                dve.wait_ge(h_blocks, count)

            def prologue(n, chain):
                b = SOURCE_BLOCKS[n]
                dve.wait_ge(x_loaded[b // 2], 32)
                chain(nc.vector.tensor_copy(early_z, own(x, b)))
                layer_norm(chain, own(h[0], b), n + 1, scratch=(early_z, early_squares),
                           scale=lambda r: nc.vector.tensor_scalar(r, r, 1.0 / (1.0 - P_DROP), None, ALU.mult),
                           last=lambda: nc.vector.scalar_tensor_tensor(
                               out=own(h[0], b), in0=own(u, b), scalar=P_DROP, in1=own(h[0], b),
                               op0=ALU.is_ge, op1=ALU.mult))
                block_ended(n + 1)

            def sum_chunk(layer, n, i, c, before, after, parts, behind_rest):
                blocks = layer * BLOCKS + n
                dve.wait_ge(chunk_loaded[c % RING], chunk_uses(layer, n, i // RING) * 16)
                tiles = [ring[c % RING][:, k * COLS:(k + 1) * COLS] for k in SUMMED_TILES[layer][c]]
                if before == 0:
                    step = nc.vector.tensor_tensor(row_sum[:, :], tiles.pop(0), tiles.pop(0), ALU.add)
                else:
                    if behind_rest:
                        dve.wait_ge(rest_summed, 2 * blocks + 3)
                    else:
                        dve.wait_ge(chunk_summed, blocks * CHUNKS + RING + before)
                    step = nc.vector.tensor_tensor(row_sum[:, :], row_sum[:, :], tiles.pop(0), ALU.add)
                for tile in tiles:
                    step.then_inc(part_summed, 1)
                    parts += 1
                    dve.wait_ge(part_summed, sum(PARTS[:layer]) * BLOCKS + n * PARTS[layer] + parts)
                    step = nc.vector.tensor_tensor(row_sum[:, :], row_sum[:, :], tile, ALU.add)
                step.then_inc(chunk_summed, after - before)
                return parts

            def sum_rest(layer, n, b, before):
                blocks = layer * BLOCKS + n
                dve.wait_ge(chunk_summed, blocks * CHUNKS + RING + before)
                if layer == 0:
                    dve.wait_ge(single_loaded, (n + 1) * 16)
                    dve.wait_ge(cache_loaded, (n + 1) * 16)
                kept = [cache[:, bass.ds((b * CACHED + m) * COLS, COLS)] for m in range(CACHED)]
                for m, tile in enumerate([single[:, :], kept[0]] if layer == 0 else kept[1:]):
                    if m:
                        dve.wait_ge(rest_summed, 2 * blocks + m + 1)
                    nc.vector.tensor_tensor(row_sum[:, :], row_sum[:, :], tile, ALU.add).then_inc(rest_summed, 1)

            def sum_tiles(layer, n, b, first):
                order = FIRST_ORDER if first else LATER_ORDER
                last = max(i for i, c in enumerate(order) if SUMMED_TILES[layer][c])
                before = parts = 0
                behind_rest = False
                for i, c in enumerate(order):
                    if i == REST_AT:
                        sum_rest(layer, n, b, before)
                        behind_rest = True
                    if layer == 0 and first and i in PROLOGUE_AT:
                        for k in PROLOGUE_AT[i]:
                            prologue(k, Chain(FIRST_STEPS + k * PROLOGUE_STEPS))
                    if SUMMED_TILES[layer][c]:
                        after = CHUNKS if i == last else i + 1
                        parts = sum_chunk(layer, n, i, c, before, after, parts, behind_rest)
                        behind_rest = False
                        before = after
                dve.wait_ge(chunk_summed, (layer * BLOCKS + n + 1) * CHUNKS + RING)

            def epilogue(layer, n, b, chain, roots):
                blocks = layer * BLOCKS + n
                xs, hs = own(x, b), own(h[(layer + 1) % 2], b)
                z, z3, Z3, s3 = z_sb, by_tile(z_sb), by_tile(Z[:, :]), by_tile(squares)
                deg, rsq = (a[:, bass.ds(b * BLOCK_TILES, BLOCK_TILES)] for a in (degree, deg_rsqrt))
                lo, hi = slice(0, BLOCK_TILES), slice(BLOCK_TILES, 2 * BLOCK_TILES)
                dve.wait_ge(z_done, blocks + 1)
                if layer == 0:
                    copy(chain, deg, DEG[:, lo])
                    new_state(chain, xs, Z[:, :])
                    layer_norm(chain, hs, roots + 1)
                elif layer == 1:
                    chain(nc.vector.scalar_tensor_tensor(out=deg, in0=DEG[:, lo], scalar=1.0, in1=deg,
                                                         op0=ALU.add, op1=ALU.add))
                    chain(nc.vector.tensor_scalar(inv_deg[:, :], deg, 1.0, None, ALU.max))
                    chain(nc.vector.reciprocal(inv_deg[:, :], inv_deg[:, :]))
                    chain(nc.vector.tensor_tensor(z3, Z3, spread(inv_deg[:, :]), ALU.mult))
                    add(chain, z, TOP[:, :], z)
                    add(chain, z3, z3, bias[:, :].unsqueeze(1).to_broadcast([P, BLOCK_TILES, F]))
                    chain(nc.vector.scalar_tensor_tensor(out=squares, in0=z, scalar=0.0, in1=z,
                                                         op0=ALU.max, op1=ALU.mult))
                    chain(nc.vector.tensor_reduce(mean[:, :], s3, X, ALU.add))
                    chain(nc.vector.tensor_scalar(to_root[:, lo], mean[:, :], L2_EPS ** 2, None, ALU.max))
                    nc.vector.tensor_scalar(to_root[:, hi], deg, LEAST_DEGREE, None,
                                            ALU.max).then_inc(root_asked, 1)
                    dve.wait_ge(root_done, roots + 1)
                    chain(nc.vector.reciprocal(inverse[:, :], rooted[:, :]))
                    chain(nc.vector.scalar_tensor_tensor(out=rsq, in0=deg, scalar=0.0, in1=inverse[:, hi],
                                                         op0=ALU.is_gt, op1=ALU.mult))
                    chain(nc.vector.scalar_tensor_tensor(out=z3, in0=z3, scalar=0.0,
                                                         in1=spread(inverse[:, lo]), op0=ALU.max, op1=ALU.mult))
                    new_state(chain, xs, z)
                    layer_norm(chain, hs, roots + 2,
                               scale=lambda r: nc.vector.tensor_tensor(r, r, rsq, ALU.mult))
                elif layer == 2:
                    chain(nc.vector.tensor_tensor(z3, Z3, spread(rsq), ALU.mult))
                    new_state(chain, xs, z)
                    layer_norm(chain, hs, roots + 1)
                else:
                    chain(nc.vector.reciprocal(inv_deg[:, :], deg))
                    chain(nc.vector.tensor_tensor(z3, Z3, spread(inv_deg[:, :]), ALU.mult))
                    add(chain, z, TOP[:, :], z)
                    nc.vector.tensor_tensor(xs, z, xs, ALU.add).then_inc(h_blocks, 1)

            def one_block(layer, n, b, first, steps, roots):
                if SUMS_DEGREE[layer]:
                    sum_tiles(layer, n, b, first)
                chain = Chain(steps + n * EPILOGUE_STEPS[layer])
                epilogue(layer, n, b, chain, roots + n * EPILOGUE_ROOTS[layer])
                block_ended((layer + 1) * BLOCKS + n + 1)
                assert chain.steps == EPILOGUE_STEPS[layer], (layer, chain.steps)

            steps, roots = FIRST_STEPS + BLOCKS * PROLOGUE_STEPS, BLOCKS
            for layer in range(LAYERS):
                if layer == 1:
                    dve.wait_ge(weights_loaded, 9 * 16)
                one_block(layer, 0, place_of(layer, 0), True, steps, roots)
                with dve.Fori(1, BLOCKS) as n:
                    one_block(layer, n, dve.snap(place_of(layer, n)), False, steps, roots)
                steps += BLOCKS * EPILOGUE_STEPS[layer]
                roots += BLOCKS * EPILOGUE_ROOTS[layer]


def kernel(x, adj, L0_gnn_u, L1_gnn_W, L1_gnn_b, L2_gnn_W, L3_gnn_W):
    import numpy as np
    import concourse.bacc as bacc
    from concourse.bass_utils import run_bass_kernel_spmd

    a = np.asarray(adj).reshape(P, BLOCKS, BLOCK_TILES, P, TILES).transpose(1, 4, 3, 2, 0)
    stream = a[:, SOURCES].reshape(BLOCKS, CHUNKS, CHUNK_TILES, P, COLS).transpose(0, 1, 3, 2, 4)
    stream = stream[:, LATER_ORDER]
    cached = a[:, KEPT].reshape(BLOCKS, CACHED, P, COLS).transpose(0, 2, 1, 3)
    arrays = {
        "x_in": np.asarray(x).reshape(P, TILES * F),
        "stream_in": stream.reshape(BLOCKS, CHUNKS, P, CHUNK_TILES * COLS),
        "single_in": a[:, SINGLE].reshape(BLOCKS, P, COLS),
        "cached_in": cached.reshape(BLOCKS, P, CACHED * COLS),
        "u_in": np.asarray(L0_gnn_u).reshape(P, TILES * F),
        "w1_in": np.asarray(L1_gnn_W),
        "b1_in": np.asarray(L1_gnn_b).reshape(1, F),
        "w2_in": np.asarray(L2_gnn_W),
        "w3_in": np.asarray(L3_gnn_W).T,
    }
    arrays = {name: np.ascontiguousarray(v) for name, v in arrays.items()}
    nc = bacc.Bacc("TRN2", target_bir_lowering=False, num_devices=1, dynamic_dma_scratch_size=2048)
    args = [nc.dram_tensor(name, v.shape, mybir.dt.from_np(v.dtype), kind="ExternalInput").ap()
            for name, v in arrays.items()]
    out = nc.dram_tensor("x_out", (P, TILES * F), mybir.dt.float32, kind="ExternalOutput").ap()
    gnn_stack(nc, *args, out)
    got = run_bass_kernel_spmd(nc, [arrays], core_ids=[0])
    return got.results[0]["x_out"].reshape(N, F)
```
